# Optimizing a Trainium2 kernel written in Bass

```python
import numpy as np
import jax
import jax.numpy as jnp

def _softmax(x, axis=-1):
    return jax.nn.softmax(x, axis=axis)

def _gelu(x):
    return jax.nn.gelu(x, approximate=True)

def _silu(x):
    return jax.nn.silu(x)

def _sigmoid(x):
    return jax.nn.sigmoid(x)

def _layernorm(x, axis=-1, eps=1e-05):
    m = jnp.mean(x, axis=axis, keepdims=True)
    v = jnp.var(x, axis=axis, keepdims=True)
    return (x - m) / jnp.sqrt(v + eps)

def _scatter_add(tgt, idx, src, axis=0):
    return tgt.at[idx].add(src)

def _segment_sum(src, seg, n):
    return jax.ops.segment_sum(src, seg, n)
kernel_name = 'mk_adaln_ffn_d2_seqx_r4_a3680b'

def setup_inputs(seed: int=0):
    np.random.seed(seed)
    _w = jnp.asarray

    def _rec_inputs():
        import jax
        import jax.numpy as jnp
        _rk = jax.random.key(seed)
        x = -0.000125 + 0.9999 * jax.random.normal(jax.random.fold_in(_rk, 1), (8, 256, 1024), jnp.float32)
        _lenS = 256 - jax.random.randint(jax.random.fold_in(_rk, 7), (8,), 0, max(1, 256 // 4) + 1, jnp.int32)
        _lenS2 = 256 - jax.random.randint(jax.random.fold_in(_rk, 8), (8,), 0, max(1, 256 // 4) + 1, jnp.int32)
        itok_B_1_7 = jax.random.randint(jax.random.fold_in(_rk, 11), (8,), 1, 8, jnp.int32)
        itok_B_6_15 = jax.random.randint(jax.random.fold_in(_rk, 12), (8,), 6, 16, jnp.int32)
        return (x, itok_B_1_7, itok_B_6_15)
    x, itok_B_1_7, itok_B_6_15 = _rec_inputs()

    def _L0_cond_setup():
        import jax, jax.numpy as jnp
        import numpy as np
        B, S, D_IN, D_OUT = (4, 512, 1024, 1024)
        N_ADAPTERS, MAX_RANK = (8, 16)
        key = jax.random.key(seed)
        ks = jax.random.split(key, 7)
        x = jax.random.normal(ks[0], (B, S, D_IN), dtype=jnp.float32)
        weight = jax.random.normal(ks[1], (D_OUT, D_IN), dtype=jnp.float32) * (1.0 / np.sqrt(D_IN))
        bias = jax.random.normal(ks[2], (D_OUT,), dtype=jnp.float32) * 0.01
        lora_a_weights = jax.random.normal(ks[3], (N_ADAPTERS, MAX_RANK, D_IN), dtype=jnp.float32) * (1.0 / np.sqrt(D_IN))
        lora_b_weights = jax.random.normal(ks[4], (N_ADAPTERS, D_OUT, MAX_RANK), dtype=jnp.float32) * 0.02
        scaling_factors = jax.random.uniform(ks[5], (N_ADAPTERS,), dtype=jnp.float32, minval=0.5, maxval=2.0)
        adapter_id = jax.random.randint(ks[6], (B,), 0, N_ADAPTERS, dtype=jnp.int64)
        return {'x': x, 'weight': weight, 'bias': bias, 'lora_a_weights': lora_a_weights, 'lora_b_weights': lora_b_weights, 'scaling_factors': scaling_factors, 'adapter_id': adapter_id}
    _L0_cond_all = _L0_cond_setup()
    _L0_cond_in = {k: v for k, v in _L0_cond_all.items() if k in ('weight', 'bias', 'lora_a_weights', 'lora_b_weights', 'scaling_factors')}
    del _L0_cond_all

    def _L0_ffn_setup():
        import jax, jax.numpy as jnp
        import numpy as np
        B, S, D, O, E, R = (2, 1024, 1024, 1024, 8, 16)
        TOP_K = 2
        SCALING = 32.0 / 16.0
        key = jax.random.key(seed)
        k = jax.random.split(key, 6)
        x = jax.random.normal(k[0], (B, S, D), dtype=jnp.float32)
        W_base = jax.random.normal(k[1], (O, D), dtype=jnp.float32) * 0.02
        b_base = jax.random.normal(k[2], (O,), dtype=jnp.float32) * 0.02
        W_router = jax.random.normal(k[3], (E, D), dtype=jnp.float32) * 0.01
        lora_A = jax.random.normal(k[4], (E, R, D), dtype=jnp.float32) * (1.0 / np.sqrt(D))
        lora_B = jax.random.normal(k[5], (E, O, R), dtype=jnp.float32) * 0.02
        return {'x': x, 'W_base': W_base, 'b_base': b_base, 'W_router': W_router, 'lora_A': lora_A, 'lora_B': lora_B}
    _L0_ffn_all = _L0_ffn_setup()
    _L0_ffn_in = {k: v for k, v in _L0_ffn_all.items() if k in ('W_base', 'b_base', 'W_router', 'lora_A', 'lora_B')}
    del _L0_ffn_all

    def _L1_cond_setup():
        import jax, jax.numpy as jnp
        import numpy as np
        B, S, D_IN, D_OUT = (4, 512, 1024, 1024)
        RANK, MAX_LORAS = (16, 32)
        key = jax.random.key(seed)
        ks = jax.random.split(key, 6)
        x = jax.random.normal(ks[0], (B, S, D_IN), dtype=jnp.float32)
        adapter_ids = jax.random.randint(ks[1], (B,), 0, MAX_LORAS)
        base_weight = jax.random.normal(ks[2], (D_OUT, D_IN), dtype=jnp.float32) * D_IN ** (-0.5)
        base_bias = jax.random.normal(ks[3], (D_OUT,), dtype=jnp.float32) * 0.01
        lora_A_w = jax.random.normal(ks[4], (MAX_LORAS, RANK, D_IN), dtype=jnp.float32) * D_IN ** (-0.5)
        lora_B_w = jax.random.normal(ks[5], (MAX_LORAS, D_OUT, RANK), dtype=jnp.float32) * RANK ** (-0.5)
        return {'x': x, 'adapter_ids': adapter_ids, 'base_weight': base_weight, 'base_bias': base_bias, 'lora_A_w': lora_A_w, 'lora_B_w': lora_B_w}
    _L1_cond_all = _L1_cond_setup()
    _L1_cond_in = {k: v for k, v in _L1_cond_all.items() if k in ('base_weight', 'base_bias', 'lora_A_w', 'lora_B_w')}
    del _L1_cond_all

    def _L1_ffn_setup():
        import jax, jax.numpy as jnp
        import numpy as np
        R = 16
        ALPHA = 32
        SCALING = ALPHA / R
        E = 8
        TOP_K = 2
        key = jax.random.key(seed)
        ks = jax.random.split(key, 5)
        B, S, D = (4, 512, 1024)
        x = jax.random.normal(ks[0], (B, S, D), dtype=jnp.float32)
        base_W = jax.random.normal(ks[1], (D, D), dtype=jnp.float32) * 0.02
        router_W = jax.random.normal(ks[2], (E, D), dtype=jnp.float32) * 0.02
        lora_A = jax.random.normal(ks[3], (E, D, R), dtype=jnp.float32) * 0.02
        lora_B = jax.random.normal(ks[4], (E, R, D), dtype=jnp.float32) * 0.02
        return {'x': x, 'base_W': base_W, 'router_W': router_W, 'lora_A': lora_A, 'lora_B': lora_B}
    _L1_ffn_all = _L1_ffn_setup()
    _L1_ffn_in = {k: v for k, v in _L1_ffn_all.items() if k in ('base_W', 'router_W', 'lora_A', 'lora_B')}
    del _L1_ffn_all
    return {'x': x, 'itok_B_1_7': itok_B_1_7, 'itok_B_6_15': itok_B_6_15, 'L0_cond_weight': _L0_cond_in['weight'], 'L0_cond_bias': _L0_cond_in['bias'], 'L0_cond_lora_a_weights': _L0_cond_in['lora_a_weights'], 'L0_cond_lora_b_weights': _L0_cond_in['lora_b_weights'], 'L0_cond_scaling_factors': _L0_cond_in['scaling_factors'], 'L0_ffn_W_base': _L0_ffn_in['W_base'], 'L0_ffn_b_base': _L0_ffn_in['b_base'], 'L0_ffn_W_router': _L0_ffn_in['W_router'], 'L0_ffn_lora_A': _L0_ffn_in['lora_A'], 'L0_ffn_lora_B': _L0_ffn_in['lora_B'], 'L1_cond_base_weight': _L1_cond_in['base_weight'], 'L1_cond_base_bias': _L1_cond_in['base_bias'], 'L1_cond_lora_A_w': _L1_cond_in['lora_A_w'], 'L1_cond_lora_B_w': _L1_cond_in['lora_B_w'], 'L1_ffn_base_W': _L1_ffn_in['base_W'], 'L1_ffn_router_W': _L1_ffn_in['router_W'], 'L1_ffn_lora_A': _L1_ffn_in['lora_A'], 'L1_ffn_lora_B': _L1_ffn_in['lora_B']}

def reference(x, itok_B_1_7, itok_B_6_15, L0_cond_weight, L0_cond_bias, L0_cond_lora_a_weights, L0_cond_lora_b_weights, L0_cond_scaling_factors, L0_ffn_W_base, L0_ffn_b_base, L0_ffn_W_router, L0_ffn_lora_A, L0_ffn_lora_B, L1_cond_base_weight, L1_cond_base_bias, L1_cond_lora_A_w, L1_cond_lora_B_w, L1_ffn_base_W, L1_ffn_router_W, L1_ffn_lora_A, L1_ffn_lora_B):
    import jax
    import jax.numpy as jnp

    def _L0_cond_ref(x, weight, bias, lora_a_weights, lora_b_weights, scaling_factors, adapter_id):
        import jax, jax.numpy as jnp
        import numpy as np
        B, S, D_IN, D_OUT = (4, 512, 1024, 1024)
        N_ADAPTERS, MAX_RANK = (8, 16)
        base = jnp.einsum('bsi,oi->bso', x, weight) + bias
        a_sel = lora_a_weights[adapter_id]
        b_sel = lora_b_weights[adapter_id]
        scale = scaling_factors[adapter_id]
        low = jnp.einsum('bsi,bri->bsr', x, a_sel)
        delta = jnp.einsum('bsr,bor->bso', low, b_sel)
        return base + scale[:, None, None] * delta

    def _L0_ffn_ref(x, W_base, b_base, W_router, lora_A, lora_B):
        import jax, jax.numpy as jnp
        import numpy as np
        B, S, D, O, E, R = (2, 1024, 1024, 1024, 8, 16)
        TOP_K = 2
        SCALING = 32.0 / 16.0
        d = x.shape[-1]
        n_experts = W_router.shape[0]
        xf = x.reshape(-1, d)
        logits = xf @ W_router.T
        probs = jax.nn.softmax(logits, axis=-1)
        topk_p, topk_i = jax.lax.top_k(probs, TOP_K)
        topk_p = topk_p / jnp.sum(topk_p, axis=-1, keepdims=True)
        w = jnp.sum(jax.nn.one_hot(topk_i, n_experts, dtype=xf.dtype) * topk_p[..., None], axis=1)
        h = jnp.einsum('td,erd->ter', xf, lora_A)
        lora_out = jnp.einsum('ter,eor,te->to', h, lora_B, w) * SCALING
        base = x @ W_base.T + b_base
        return base + lora_out.reshape(x.shape[:-1] + (W_base.shape[0],))

    def _L1_cond_ref(x, adapter_ids, base_weight, base_bias, lora_A_w, lora_B_w):
        import jax, jax.numpy as jnp
        import numpy as np
        B, S, D_IN, D_OUT = (4, 512, 1024, 1024)
        RANK, MAX_LORAS = (16, 32)
        result = jnp.einsum('bsd,od->bso', x, base_weight) + base_bias
        A = lora_A_w[adapter_ids]
        Bw = lora_B_w[adapter_ids]
        h = jnp.einsum('bsd,brd->bsr', x, A)
        lora_out = jnp.einsum('bsr,bor->bso', h, Bw)
        result = result + lora_out
        return result.astype(x.dtype)

    def _L1_ffn_ref(x, base_W, router_W, lora_A, lora_B):
        import jax, jax.numpy as jnp
        import numpy as np
        R = 16
        ALPHA = 32
        SCALING = ALPHA / R
        E = 8
        TOP_K = 2
        base = jnp.einsum('bsd,od->bso', x, base_W)
        logits = jnp.einsum('bsd,ed->bse', x, router_W)
        probs = jax.nn.softmax(logits.astype(jnp.float32), axis=-1)
        top_vals, top_idx = jax.lax.top_k(probs, TOP_K)
        rw = top_vals / jnp.sum(top_vals, axis=-1, keepdims=True)
        w_dense = jnp.sum(jax.nn.one_hot(top_idx, E, dtype=rw.dtype) * rw[..., None], axis=-2).astype(x.dtype)
        mid = jnp.einsum('bsd,edr->bser', x, lora_A)
        mid = mid * w_dense[..., None]
        inc = jnp.einsum('bser,erd->bsd', mid, lora_B)
        return base + inc * SCALING
    x = x + _L0_ffn_ref(_L0_cond_ref(x, L0_cond_weight, L0_cond_bias, L0_cond_lora_a_weights, L0_cond_lora_b_weights, L0_cond_scaling_factors, itok_B_1_7), L0_ffn_W_base, L0_ffn_b_base, L0_ffn_W_router, L0_ffn_lora_A, L0_ffn_lora_B)
    x = x + _L1_ffn_ref(_L1_cond_ref(x, itok_B_6_15, L1_cond_base_weight, L1_cond_base_bias, L1_cond_lora_A_w, L1_cond_lora_B_w), L1_ffn_base_W, L1_ffn_router_W, L1_ffn_lora_A, L1_ffn_lora_B)
    return x

_drawn_inputs = setup_inputs


def setup_inputs(seed=0):
    import zlib

    import numpy as np

    out = dict(_drawn_inputs(seed))
    spreads = {}
    factors = {'L0_cond_bias': 5.841, 'L0_ffn_b_base': 3.191, 'L1_cond_base_bias': 8.0}
    for name, (base, spread) in spreads.items():
        noise = np.random.default_rng([zlib.crc32(name.encode()), seed]).standard_normal(out[name].shape)
        drawn = base * np.exp(spread * noise) if base else spread * noise
        out[name] = jnp.asarray(drawn.astype(out[name].dtype))
    for name, factor in factors.items():
        out[name] = (out[name] * factor).astype(out[name].dtype)
    return out
```

```python
from contextlib import ExitStack

import concourse.bass as bass
from concourse import mybir

LAYERS = 2
D = 1024
P = 128
KT = D // P
BATCH, SEQ = 8, 256
T = BATCH * SEQ
CH = 512
NCH = T // CH
BPC = CH // SEQ
TT = CH // P
R = 16
NE = 8
ER = NE * R
EXT = D + ER + NE
OB = ((0, 388), (388, 388), (776, 384))
NOB = len(OB)
RT = KT + 1
UNITS = RT * NOB
K_ORDER = (5, 6, 7, 4, 0, 1, 2, 3)
LOW = BPC * R
ONES_ROW = 3 * LOW
STACK = ONES_ROW + 2
SROWS = STACK + NE
FREE = 1
SLOTS = 4
GROUPS = ((0, 1, 2), (3, 4, 5), (6, 7))
CHAIN = 12


def fused_layers(nc, xT, w0, ext, lb, a_tab, b_tab, scale_tab, ids, b0, b1, ident, smask, iota, rtail, out):
    f32, f32r = mybir.dt.float32, mybir.dt.float32r
    ALU = mybir.AluOpType
    ACT = mybir.ActivationFunctionType
    ds = bass.ds

    ctx = ExitStack()
    with ctx:
        sem_names = (
            "d_ids d_const d_w0a d_w0b d_lb d_adapt_a d_b d_scale d_b0 d_b1 d_bw d_stack d_bias_rows "
            "w0_hi w0_lo e_hi e_lo lb_hi lb_lo p_hi p_lo acc_zero acc_half acc_done bias_r_done bias_hi bias_lo bwr_done router_cols "
            "scale_one mul_done zero_cols "
            "pe_unit pe_brow pe_bias pe_s pe_h pe_logit pe_gate pe_out pe_xfree "
            "sx_done low_hi low_lo h_done shi_done slo_done gap_done exp_done gate_done hg_done hg_hi hg_lo "
            "x_hi x_lo resid_done out_done dve_step"
        ).split()
        S = {n: ctx.enter_context(nc.semaphore(n)) for n in sem_names}
        d_w0 = [S["d_w0a"], S["d_w0b"]]
        d_e = [ctx.enter_context(nc.semaphore(f"d_e{k}")) for k in range(KT)]
        d_x = [ctx.enter_context(nc.semaphore(f"d_x{i}")) for i in range(SLOTS)]
        d_out = [ctx.enter_context(nc.semaphore(f"d_out{i}")) for i in range(SLOTS)]

        base = -(-nc.sbuf_base // 64) * 64
        at = [base]

        def place(name, shape, dt, offset=None):
            size = 4
            for n in shape[1:]:
                size *= n
            if offset is None:
                offset = at[0]
                at[0] += -(-size // 32) * 32
            return nc.alloc_sbuf_tensor_at(name, shape, dt, offset=offset)

        E_TILE = 2 * EXT * 4
        e_at = at[0]
        e_hl = place("e_hl", [P, KT, 2, EXT], f32r)
        e_raw = place("e_raw", [P, KT, 2, EXT], f32, e_at)
        x_hl = place("x_hl", [P, KT, 2, CH], f32r, e_at)
        lb_hl = place("lb_hl", [P, 2, D], f32r, e_at + 4 * E_TILE)
        lb_raw = place("lb_raw", [P, 2, D], f32, e_at + 4 * E_TILE)
        w0_at = at[0]
        w0_hl = place("w0_hl", [P, 2, 2, D], f32r)
        w0_raw = place("w0_raw", [P, 2, 2, D], f32, w0_at)
        bias_hl = place("bias_hl", [1, 2, EXT], f32r, w0_at)
        p_hl = place("p_hl", [P, KT, 2, EXT], f32r)
        s_hl = place("s_hl", [P, KT, 2, SROWS], f32r)
        a_raw = place("a_raw", [P, BATCH, KT, R], f32)
        stack = place("stack", [STACK, D + ER], f32r)
        out_at = at[0]
        out_st = place("out_st", [P, SLOTS, CH], f32)
        acc = place("acc", [P, EXT], f32, out_at)
        x_at = at[0]
        x_st = place("x_st", [P, SLOTS, CH], f32)
        b_raw = place("b_raw", [P, BATCH, KT, R], f32, x_at)
        misc_at = at[0]
        h_sb = place("h_sb", [P, CH], f32)
        hg_at = at[0]
        hg = place("hg", [P, CH], f32)
        gates = place("gates", [P, TT, ER], f32, hg_at)
        hg_hl = place("hg_hl", [P, 2, CH], f32r)
        sx = place("sx", [SROWS, CH], f32)
        low_mv = place("low_mv", [STACK, CH], f32r)
        bw_st = place("bw_st", [P, NOB, 2, OB[0][1]], f32r, misc_at)
        ident_sb = place("ident_sb", [P, P], f32)
        iota_sb = place("iota_sb", [P, TT, NE], f32)
        smask_sb = place("smask_sb", [SROWS, BPC + 1], f32)
        ones_sb = place("ones_sb", [P, 1], f32)
        scale_sb = place("scale_sb", [SROWS, BATCH], f32)
        mul_sb = place("mul_sb", [SROWS, BATCH], f32)
        rlog = place("rlog", [SROWS, NE], f32)
        bwr = place("bwr", [P, NE], f32)
        bias_r = place("bias_r", [1, NE], f32)
        b0_sb = place("b0_sb", [P, KT], f32)
        ids_sb = place("ids_sb", [1, LAYERS * BATCH], mybir.dt.int32)
        lg = place("lg", [P, TT, NE], f32)
        top = place("top", [P, TT, 8], f32)
        top_i = place("top_i", [P, TT, 8], mybir.dt.uint32)
        top_f = place("top_f", [P, TT, 8], f32)
        gap = place("gap", [P, TT, 1], f32)
        ex = place("ex", [P, TT, 1], f32)
        den = place("den", [P, TT, 1], f32)
        wa = place("wa", [P, TT, 1], f32)
        wb = place("wb", [P, TT, 1], f32)
        ma = place("ma", [P, TT, NE], f32)
        mb = place("mb", [P, TT, NE], f32)
        assert at[0] <= nc.sbuf_usable_end, at[0] - nc.sbuf_usable_end
        ps = ctx.enter_context(nc.psum_tensor("ps", [P, 8, 512], f32))
        S_BANK, H_BANK = 6, 7

        x1 = nc.dram_tensor("x1_scratch", (D, T), f32, kind="Internal").ap()
        bw_dram = nc.dram_tensor("bw_scratch", (LAYERS, P, 2, EXT), f32, kind="Internal").ap()
        bwr_dram = nc.dram_tensor("bwr_scratch", (LAYERS, P, NE), f32, kind="Internal").ap()
        src_of, dst_of = (xT, x1), (x1, out)

        def x_after(k):
            return ((k + 1) * 2 * CH * 4 - 1) // E_TILE + 1

        def by_tile(v):
            return v.rearrange("p (k b r) -> p k b r", k=KT, b=BATCH)

        block = ctx.enter_context(nc.Block())

        @block.sync
        def _(sp):
            def load_first(l):
                if l:
                    sp.wait_ge(S["pe_unit"], UNITS * l)
                    sp.wait_ge(S["d_bias_rows"], 48 * l)
                sp.dma_start(w0_raw[:, 0, 1, :], w0[l, 0]).then_inc(d_w0[0], 16)
                for k in K_ORDER[:3]:
                    sp.dma_start(e_raw[:, k, 1, :], ext[l, k * P:(k + 1) * P, :]).then_inc(d_e[k], 16)

            def load_fold(l):
                for k in K_ORDER[3:]:
                    if l and k == 4:
                        sp.wait_ge(S["pe_out"], KT * NCH * l)
                    if l and k == K_ORDER[4]:
                        sp.wait_ge(S["pe_xfree"], KT * NCH * l)
                        sp.wait_ge(S["resid_done"], KT * NCH * l)
                    sp.dma_start(e_raw[:, k, 1, :], ext[l, k * P:(k + 1) * P, :]).then_inc(d_e[k], 16)
                sp.dma_start(w0_raw[:, 1, 1, :], w0[l, 1]).then_inc(d_w0[1], 16)
                if l == 0:
                    for dst, src in ((ident_sb, ident), (iota_sb, iota), (smask_sb, smask), (rlog, rtail)):
                        sp.dma_start(dst[:], src).then_inc(S["d_const"], 16)
                sp.dma_start(b0_sb[:], b0[l]).then_inc(S["d_b0"], 16)
                sp.wait_ge(S["acc_zero"], l + 1)
                sp.dma_start(acc[0:1, :], b1[l]).then_inc(S["d_b1"], 16)
                if l == 0:
                    sp.wait_ge(S["d_ids"], 16)
                first, count = ((0, 8), (8, 32))[l]
                who = [sp.value_load(ids_sb[0:1, BATCH * l + b:BATCH * l + b + 1], min_val=0, max_val=count - 1)
                       for b in range(BATCH)]
                a_l, b_l, s_l = (tab[first:first + count] for tab in (a_tab, b_tab, scale_tab))
                sp.wait_ge(S["scale_one"], l + 1)
                if l:
                    sp.wait_ge(S["slo_done"], NCH * l)
                    sp.wait_ge(S["x_lo"], KT * NCH * l)
                for b in range(BATCH):
                    sp.dma_start(a_raw[:, b:b + 1, :, :].rearrange("p o k r -> p (o k r)"),
                                 a_l[ds(who[b], 1)].rearrange("o p n -> (o p) n")).then_inc(S["d_adapt_a"], 16)
                    sp.dma_start(scale_sb[0:ONES_ROW, b:b + 1],
                                 s_l[ds(who[b], 1)].broadcast_to([ONES_ROW, 1])).then_inc(S["d_scale"], 16)
                for b in range(BATCH):
                    sp.dma_start(b_raw[:, b:b + 1, :, :].rearrange("p o k r -> p (o k r)"),
                                 b_l[ds(who[b], 1)].rearrange("o p n -> (o p) n")).then_inc(S["d_b"], 16)

            def load_rows(l):
                with sp.Fori(0, (KT - 2) // 2) as pair:
                    for odd in range(2):
                        sp.wait_ge(S["pe_unit"], pair * (2 * NOB) + (UNITS * l + (1 + odd) * NOB))
                        sp.dma_start(w0_raw[:, odd, 1, :],
                                     w0[l, ds(pair * 2 + (2 + odd), 1)].rearrange("o p n -> (o p) n")
                                     ).then_inc(d_w0[odd], 16)

            def load_x(l, g, c, ks):
                for k in ks:
                    if not (isinstance(g, int) and g * KT + k < SLOTS):
                        sp.wait_ge(S["x_lo"], g * KT + (k - SLOTS + 1))
                    sp.dma_start(x_st[:, k % SLOTS, :],
                                 src_of[l][k * P:(k + 1) * P, ds(c * CH, CH)]).then_inc(d_x[k % SLOTS], 16)

            def store(l, g, c, ms):
                for m in ms:
                    sp.wait_ge(S["out_done"], g * KT + (m + 1 + FREE))
                    sp.dma_start(dst_of[l][m * P:(m + 1) * P, ds(c * CH, CH)],
                                 out_st[:, m % SLOTS, :]).then_inc(d_out[m % SLOTS], 16)

            def load_stack(l, c):
                for i, hl in enumerate((0, 1, 0)):
                    sp.dma_start(stack[i * LOW:(i + 1) * LOW, :].bitcast(f32),
                                 bw_dram[l, ds(c * LOW, LOW), hl, 0:D + ER]).then_inc(S["d_stack"], 16)
                sp.dma_start(rlog[0:LOW, :], bwr_dram[l, ds(c * LOW, LOW), :]).then_inc(S["d_stack"], 16)

            for s in range(SLOTS):
                sp.sem_inc(d_out[s], 16)
            sp.dma_start(ids_sb[:], ids).then_inc(S["d_ids"], 16)
            load_first(0)
            for l in range(LAYERS):
                g0 = NCH * l
                load_fold(l)
                load_rows(l)
                sp.wait_ge(S["w0_lo"], RT * (l + 1))
                if l:
                    for s in range(SLOTS):
                        sp.wait_ge(d_out[s], 16 * (KT // SLOTS) * NCH * l + 16)
                load_x(l, g0, 0, range(SLOTS))
                load_x(l, g0, 0, range(SLOTS, KT))
                sp.wait_ge(S["pe_brow"], (KT - 1) * l + 5)
                sp.wait_ge(S["acc_done"], KT * l + 5)
                sp.dma_start(lb_raw[:, 1, :], lb[l]).then_inc(S["d_lb"], 16)
                for ob, (o, n) in enumerate(OB):
                    sp.wait_ge(S["p_lo"], UNITS * l + KT * NOB + ob + 1)
                    sp.dma_start(bw_dram[l, :, :, o:o + n], bw_st[:, ob, :, 0:n].bitcast(f32)).then_inc(S["d_bw"], 16)
                sp.wait_ge(S["bwr_done"], l + 1)
                sp.dma_start(bwr_dram[l], bwr[:]).then_inc(S["d_bw"], 16)
                sp.wait_ge(S["bias_r_done"], l + 1)
                sp.wait_ge(S["bias_lo"], NOB * (l + 1))
                for hl in range(2):
                    sp.dma_start(stack[ONES_ROW + hl:ONES_ROW + hl + 1, :].bitcast(f32),
                                 bias_hl[:, hl, 0:D + ER].bitcast(f32)).then_inc(S["d_bias_rows"], 16)
                sp.dma_start(rlog[ONES_ROW:ONES_ROW + 1, :], bias_r[:]).then_inc(S["d_bias_rows"], 16)
                sp.wait_ge(S["d_bw"], 64 * (l + 1))
                load_stack(l, 0)

                def chunk(c, last):
                    g = c + g0
                    if last and l + 1 < LAYERS:
                        load_first(l + 1)
                    if not last:
                        load_x(l, g + 1, c + 1, range(SLOTS))
                    store(l, g, c, range(6))
                    if not last:
                        load_x(l, g + 1, c + 1, range(SLOTS, KT))
                        sp.wait_ge(S["pe_out"], g * KT + KT)
                        load_stack(l, c + 1)
                    store(l, g, c, range(6, KT))

                with sp.Fori(0, NCH - 1) as c:
                    chunk(c, False)
                chunk(NCH - 1, True)
            for s in range(SLOTS):
                sp.wait_ge(d_out[s], 16 * (KT // SLOTS) * NCH * LAYERS + 16)

        @block.tensor
        def _(pe):
            def split_product(dst, w_hi, w_lo, m_hi, m_lo, start, stop):
                nc.tensor.matmul(dst, w_hi, m_hi, start=start, stop=False)
                nc.tensor.matmul(dst, w_hi, m_lo, start=False, stop=False)
                return nc.tensor.matmul(dst, w_lo, m_hi, start=False, stop=stop)

            def fold_unit(buf, bank, k, ob, start, stop):
                o, n = OB[ob]
                w = [w0_hl[:, buf, hl, k * P:(k + 1) * P] for hl in range(2)]
                return split_product(ps[:, bank, 0:n], w[0], w[1], e_hl[:, k, 0, o:o + n], e_hl[:, k, 1, o:o + n],
                                     start, stop)

            def row_tile(l, rt, odd, reused):
                pe.wait_ge(S["w0_lo"], rt + (RT * l + 1))
                for ob in range(NOB):
                    if reused:
                        pe.wait_ge(S["p_lo"], rt * NOB + (UNITS * l + ob - 2 * NOB + 1))
                    for i, k in enumerate(K_ORDER):
                        last = fold_unit(odd, odd * NOB + ob, k, ob, i == 0, i == KT - 1)
                    last.then_inc(S["pe_unit"], 1)

            for l in range(LAYERS):
                pe.wait_ge(S["w0_lo"], RT * l + 1)
                if l:
                    pe.wait_ge(S["out_done"], KT * NCH * l + FREE)
                for i, k in enumerate(K_ORDER):
                    pe.wait_ge(S["e_lo"], KT * l + i + 1)
                    for ob in range(NOB):
                        last = fold_unit(0, ob, k, ob, i == 0, i == KT - 1)
                        if i == KT - 1:
                            last.then_inc(S["pe_unit"], 1)
                row_tile(l, 1, 1, False)
                with pe.Fori(0, (KT - 2) // 2) as pair:
                    row_tile(l, pair * 2 + 2, 0, True)
                    row_tile(l, pair * 2 + 3, 1, True)
                pe.wait_ge(S["w0_lo"], RT * (l + 1))
                pe.wait_ge(S["p_lo"], UNITS * l + 7 * NOB)
                for k in range(KT):
                    for ob in range(NOB):
                        last = fold_unit(0, ob, k, ob, k == 0, k == KT - 1)
                        if k == KT - 1:
                            last.then_inc(S["pe_unit"], 1)
                    if k < KT - 1:
                        last.then_inc(S["pe_brow"], 1)
                pe.wait_ge(S["acc_done"], KT * (l + 1))
                pe.wait_ge(S["p_lo"], UNITS * l + KT * NOB)
                for ob, (o, n) in enumerate(OB):
                    nc.tensor.matmul(ps[0:1, NOB + ob, 0:n], ones_sb[:], acc[:, o:o + n],
                                     start=True, stop=True).then_inc(S["pe_bias"], 1)
                pe.wait_ge(S["router_cols"], l + 1)
                with pe.Fori(0, NCH) as c:
                    g = c + NCH * l
                    pe.wait_ge(S["slo_done"], g + 1)
                    pe.wait_ge(S["hg_done"], g + FREE)
                    for k in range(KT):
                        pe.wait_ge(S["x_lo"], g * KT + (k + 1))
                        last = split_product(ps[0:SROWS, S_BANK, :], s_hl[:, k, 0, :], s_hl[:, k, 1, :],
                                             x_hl[:, k, 0, :], x_hl[:, k, 1, :], k == 0, k == KT - 1)
                    last.then_inc(S["pe_s"], 1)
                    pe.wait_ge(S["h_done"], g + FREE)
                    for k in range(KT):
                        split_product(ps[:, H_BANK, :], p_hl[:, k, 0, D:D + ER], p_hl[:, k, 1, D:D + ER],
                                      x_hl[:, k, 0, :], x_hl[:, k, 1, :], k == 0, False)
                    pe.wait_ge(S["low_lo"], g + 1)
                    pe.wait_ge(S["d_stack"], g * 64 + 64)
                    pe.wait_ge(S["d_bias_rows"], 48 * (l + 1))
                    nc.tensor.matmul(ps[:, H_BANK, :], stack[:, D:D + ER], low_mv[:], start=False,
                                     stop=True).then_inc(S["pe_h"], 1)
                    for t in range(TT):
                        last = nc.tensor.matmul(ps[:, S_BANK, t * NE:(t + 1) * NE], sx[:, t * P:(t + 1) * P],
                                                rlog[:], start=True, stop=True)
                    last.then_inc(S["pe_logit"], 1)

                    def main(group, freeing):
                        for k in range(KT):
                            for m in group:
                                last = split_product(ps[:, m % 6, :], p_hl[:, k, 0, m * P:(m + 1) * P],
                                                     p_hl[:, k, 1, m * P:(m + 1) * P],
                                                     x_hl[:, k, 0, :], x_hl[:, k, 1, :], k == 0, False)
                            if freeing:
                                last.then_inc(S["pe_xfree"], 1)

                    def low_and_experts(group):
                        for m in group:
                            cols = slice(m * P, (m + 1) * P)
                            nc.tensor.matmul(ps[:, m % 6, :], stack[:, cols], low_mv[:], start=False, stop=False)
                            split_product(ps[:, m % 6, :], lb_hl[:, 0, cols], lb_hl[:, 1, cols],
                                          hg_hl[:, 0, :], hg_hl[:, 1, :], False, True).then_inc(S["pe_out"], 1)

                    pe.wait_ge(S["out_done"], g * KT + FREE)
                    pe.wait_ge(S["p_lo"], UNITS * (l + 1))
                    main(GROUPS[0], False)
                    pe.wait_ge(S["gate_done"], g + 1)
                    for t in range(TT):
                        last = nc.tensor.matmul(ps[:, S_BANK, t * P:(t + 1) * P],
                                                gates[:, t, :],
                                                ident_sb[:], start=True, stop=True)
                    last.then_inc(S["pe_gate"], 1)
                    pe.wait_ge(S["bias_lo"], NOB * (l + 1))
                    main(GROUPS[1], False)
                    pe.wait_ge(S["hg_lo"], g + 1)
                    pe.wait_ge(S["lb_lo"], l + 1)
                    low_and_experts(GROUPS[0])
                    low_and_experts(GROUPS[1])
                    pe.wait_ge(S["out_done"], g * KT + (2 + FREE))
                    main(GROUPS[2], True)
                    low_and_experts(GROUPS[2])

        @block.scalar
        def _(act):
            def w0_split(l, buf, loads):
                act.wait_ge(d_w0[buf], loads)
                nc.scalar.copy(w0_hl[:, buf, 0, :], w0_raw[:, buf, 1, :]).then_inc(S["w0_hi"], 1)

            def e_split(l, i):
                k = K_ORDER[i]
                act.wait_ge(d_e[k], 16 * (l + 1))
                nc.scalar.copy(e_hl[:, k, 0, :], e_raw[:, k, 1, :]).then_inc(S["e_hi"], 1)

            def first(l):
                w0_split(l, 0, 16 * (KT // 2) * l + 16)
                for i in range(3):
                    e_split(l, i)

            def p_evac(l, rt, odd):
                for ob, (o, n) in enumerate(OB):
                    act.wait_ge(S["pe_unit"], rt * NOB + (UNITS * l + ob + 1))
                    act.reg_add(act_idle, act_idle, 1)
                    nc.scalar.copy(p_hl[:, ds(rt, 1), 0, o:o + n],
                                   ps[:, odd * NOB + ob, 0:n].unsqueeze(1)).then_inc(S["p_hi"], 1)

            def step(l, rt, odd):
                p_evac(l, rt, odd)
                w0_split(l, odd, rt * 8 + (16 * (KT // 2) * l + (24 if odd else 32)))

            act.sem_inc(S["h_done"], FREE)
            act_idle = act.alloc_register("act_idle")
            act.reg_mov(act_idle, 0)
            first(0)
            for l in range(LAYERS):
                for i in range(3, KT):
                    e_split(l, i)
                w0_split(l, 1, 16 * (KT // 2) * l + 16)
                act.wait_ge(S["d_const"], 64)
                act.wait_ge(S["d_adapt_a"], 16 * BATCH * (l + 1))
                if l:
                    act.wait_ge(S["pe_s"], NCH * l)
                else:
                    act.wait_ge(S["zero_cols"], 1)

                def s_split(b):
                    for i in range(3):
                        last = nc.scalar.copy(
                            s_hl[:, :, 0, i * LOW:(i + 1) * LOW].rearrange("p k (j r) -> p k j r", j=BPC),
                            a_raw[:, ds(b, BPC), :, :].rearrange("p j k r -> p k j r"))
                    last.then_inc(S["shi_done"], 1)

                s_split(0)
                step(l, 0, 0)
                step(l, 1, 1)
                with act.Fori(0, 2) as pair:
                    step(l, pair * 2 + 2, 0)
                    step(l, pair * 2 + 3, 1)
                p_evac(l, KT - 2, 0)
                act.wait_ge(S["d_b"], 16 * BATCH * (l + 1))
                nc.scalar.copy(by_tile(w0_hl[:, 0, 0, :]),
                               b_raw[:].rearrange("p b k r -> p k b r")).then_inc(S["w0_hi"], 1)
                p_evac(l, KT - 1, 1)

                def x_split(g, k, fresh):
                    act.wait_ge(d_x[k % SLOTS], g * (16 * KT // SLOTS) + 16 * (k // SLOTS + 1))
                    if fresh:
                        act.wait_ge(S["pe_brow"], (KT - 1) * l + x_after(k))
                        act.wait_ge(S["acc_done"], KT * l + x_after(k))
                    else:
                        act.wait_ge(S["pe_xfree"], (g - 1) * KT + (k + 1))
                        act.wait_ge(S["resid_done"], (g - 1) * KT + (k + 1))
                    nc.scalar.copy(x_hl[:, k, 0, :], x_st[:, k % SLOTS, :]).then_inc(S["x_hi"], 1)

                for k in range(KT):
                    x_split(NCH * l, k, True)
                for ob, (o, n) in enumerate(OB):
                    act.wait_ge(S["pe_unit"], UNITS * l + KT * NOB + ob + 1)
                    nc.scalar.copy(bw_st[:, ob, 0, 0:n], ps[:, ob, 0:n]).then_inc(S["p_hi"], 1)
                act.wait_ge(S["pe_unit"], UNITS * (l + 1))
                for ob, (o, n) in enumerate(OB):
                    act.wait_ge(S["pe_bias"], NOB * l + ob + 1)
                    nc.scalar.copy(bias_hl[:, 0, o:o + n], ps[0:1, NOB + ob, 0:n]).then_inc(S["bias_hi"], 1)
                act.wait_ge(S["d_lb"], 16 * (l + 1))
                nc.scalar.copy(lb_hl[:, 0, :], lb_raw[:, 1, :]).then_inc(S["lb_hi"], 1)

                def chunk(c, last):
                    g = c + NCH * l
                    act.wait_ge(S["sx_done"], g + 1)
                    nc.scalar.copy(low_mv[:], sx[0:STACK, :]).then_inc(S["low_hi"], 1)
                    if not last:
                        s_split(c * BPC + BPC)
                    act.wait_ge(S["pe_h"], g + 1)
                    nc.scalar.copy(h_sb[:], ps[:, H_BANK, :]).then_inc(S["h_done"], 1)
                    act.wait_ge(S["gap_done"], g + 1)
                    nc.scalar.activation(ex[:], gap[:], ACT.Exp).then_inc(S["exp_done"], 1)
                    act.wait_ge(S["hg_done"], g + (1 + FREE))
                    nc.scalar.copy(hg_hl[:, 0, :], hg[:]).then_inc(S["hg_hi"], 1)
                    if not last:
                        for k in range(KT):
                            x_split(g + 1, k, False)

                with act.Fori(0, NCH - 1) as c:
                    chunk(c, False)
                chunk(NCH - 1, True)
                if l + 1 < LAYERS:
                    first(l + 1)

        @block.vector
        def _(dve):
            def sub(dst, a, b):
                return nc.vector.tensor_tensor(dst, a, b, ALU.subtract)

            def w0_split(l, rt, buf):
                dve.wait_ge(S["w0_hi"], rt + (RT * l + 1))
                sub(w0_hl[:, buf, 1, :], w0_raw[:, buf, 1, :],
                    w0_hl[:, buf, 0, :].bitcast(f32)).then_inc(S["w0_lo"], 1)

            def e_split(l, i):
                k = K_ORDER[i]
                dve.wait_ge(S["e_hi"], KT * l + i + 1)
                sub(e_hl[:, k, 1, :], e_raw[:, k, 1, :], e_hl[:, k, 0, :].bitcast(f32)).then_inc(S["e_lo"], 1)

            def first(l):
                w0_split(l, 0, 0)
                for i in range(3):
                    e_split(l, i)

            def acc_row(l, k):
                for hl in range(2):
                    if hl:
                        dve.wait_ge(S["acc_half"], k + (KT * l + 1))
                    elif not (isinstance(k, int) and k + KT * l == 0):
                        dve.wait_ge(S["acc_done"], k + KT * l)
                    ins = nc.vector.scalar_tensor_tensor(
                        acc[:].unsqueeze(1), e_hl[:, ds(k, 1), hl, :].bitcast(f32), b0_sb[:, ds(k, 1)],
                        acc[:].unsqueeze(1), op0=ALU.mult, op1=ALU.add)
                    ins.then_inc(S["acc_done" if hl else "acc_half"], 1)

            def p_evac(l, rt, odd):
                for ob, (o, n) in enumerate(OB):
                    dve.wait_ge(S["p_hi"], rt * NOB + (UNITS * l + ob + 1))
                    sub(p_hl[:, ds(rt, 1), 1, o:o + n], ps[:, odd * NOB + ob, 0:n].unsqueeze(1),
                        p_hl[:, ds(rt, 1), 0, o:o + n].bitcast(f32)).then_inc(S["p_lo"], 1)

            def step(l, rt, odd):
                acc_row(l, rt - 1)
                p_evac(l, rt, odd)
                w0_split(l, rt + 2, odd)

            dve.sem_inc(S["hg_done"], FREE)
            dve.sem_inc(S["out_done"], FREE)
            nc.vector.memset(ones_sb[:], 1.0)
            nc.vector.memset(s_hl[:].bitcast(f32), 0.0).then_inc(S["zero_cols"], 1)
            nc.vector.memset(scale_sb[:], 1.0).then_inc(S["scale_one"], 1)
            first(0)
            for l in range(LAYERS):
                for i in range(3, KT):
                    e_split(l, i)
                w0_split(l, 1, 1)

                def s_split(g, b):
                    dve.wait_ge(S["shi_done"], g + 1)
                    for i in range(3):
                        v = [s_hl[:, :, hl, i * LOW:(i + 1) * LOW].rearrange("p k (j r) -> p k j r", j=BPC)
                             for hl in range(2)]
                        last = sub(v[1], a_raw[:, ds(b, BPC), :, :].rearrange("p j k r -> p k j r"),
                                   v[0].bitcast(f32))
                    last.then_inc(S["slo_done"], 1)

                s_split(NCH * l, 0)
                dve.wait_ge(S["d_const"], 64)
                dve.wait_ge(S["d_scale"], 16 * BATCH * (l + 1))
                for j in range(BPC):
                    last = nc.vector.tensor_scalar(
                        mul_sb[:].rearrange("p (c j) -> p c j", j=BPC)[:, :, j],
                        scale_sb[:].rearrange("p (c j) -> p c j", j=BPC)[:, :, j],
                        smask_sb[:, j:j + 1], None, ALU.mult)
                last.then_inc(S["mul_done"], 1)
                if l == 0:
                    dve.wait_ge(S["mul_done"], 1)
                    nc.vector.memset(scale_sb[:], 1.0).then_inc(S["scale_one"], 1)
                dve.wait_ge(S["d_b0"], 16 * (l + 1))
                dve.wait_ge(S["d_b1"], 16 * (l + 1))
                dve.wait_ge(S["e_lo"], KT * (l + 1))
                p_evac(l, 0, 0)
                w0_split(l, 2, 0)
                step(l, 1, 1)
                with dve.Fori(0, 2) as pair:
                    step(l, pair * 2 + 2, 0)
                    step(l, pair * 2 + 3, 1)
                acc_row(l, KT - 3)
                p_evac(l, KT - 2, 0)
                dve.wait_ge(S["w0_hi"], RT * (l + 1))
                sub(by_tile(w0_hl[:, 0, 1, :]), b_raw[:].rearrange("p b k r -> p k b r"),
                    by_tile(w0_hl[:, 0, 0, :]).bitcast(f32)).then_inc(S["w0_lo"], 1)
                acc_row(l, KT - 2)
                p_evac(l, KT - 1, 1)
                dve.wait_ge(S["p_lo"], UNITS * l + KT * NOB)
                nc.vector.tensor_copy(s_hl[:, :, :, STACK:SROWS],
                                      p_hl[:, :, :, D + ER:EXT]).then_inc(S["router_cols"], 1)
                acc_row(l, KT - 1)

                def x_split(g, k):
                    dve.wait_ge(S["x_hi"], g * KT + (k + 1))
                    sub(x_hl[:, k, 1, :], x_st[:, k % SLOTS, :],
                        x_hl[:, k, 0, :].bitcast(f32)).then_inc(S["x_lo"], 1)

                for k in range(KT):
                    x_split(NCH * l, k)
                for ob, (o, n) in enumerate(OB):
                    dve.wait_ge(S["p_hi"], UNITS * l + KT * NOB + ob + 1)
                    sub(bw_st[:, ob, 1, 0:n], ps[:, ob, 0:n],
                        bw_st[:, ob, 0, 0:n].bitcast(f32)).then_inc(S["p_lo"], 1)
                n = OB[-1][1]
                nc.vector.tensor_copy(bwr[:], ps[:, NOB - 1, n - NE:n]).then_inc(S["bwr_done"], 1)
                for ob, (o, n) in enumerate(OB):
                    dve.wait_ge(S["bias_hi"], NOB * l + ob + 1)
                    sub(bias_hl[:, 1, o:o + n], ps[0:1, NOB + ob, 0:n],
                        bias_hl[:, 0, o:o + n].bitcast(f32)).then_inc(S["bias_lo"], 1)
                nc.vector.tensor_copy(bias_r[:], ps[0:1, 2 * NOB - 1, n - NE:n]).then_inc(S["bias_r_done"], 1)
                dve.wait_ge(S["lb_hi"], l + 1)
                sub(lb_hl[:, 1, :], lb_raw[:, 1, :], lb_hl[:, 0, :].bitcast(f32)).then_inc(S["lb_lo"], 1)
                dve.wait_ge(S["d_bw"], 64 * (l + 1))
                dve.wait_ge(S["mul_done"], l + 1)

                def chunk(c, last):
                    g = c + NCH * l
                    count = [0]

                    def chain(ins, wait=True):
                        ins.then_inc(S["dve_step"], 1)
                        count[0] += 1
                        if wait:
                            dve.wait_ge(S["dve_step"], g * CHAIN + count[0])

                    dve.wait_ge(S["pe_s"], g + 1)
                    for j in range(BPC):
                        ins = nc.vector.tensor_scalar(
                            sx[:, j * SEQ:(j + 1) * SEQ], ps[0:SROWS, S_BANK, j * SEQ:(j + 1) * SEQ],
                            mul_sb[:, ds(c * BPC + j, 1)], smask_sb[:, BPC:BPC + 1], ALU.mult, ALU.add)
                    ins.then_inc(S["sx_done"], 1)
                    dve.wait_ge(S["low_hi"], g + 1)
                    third = slice(2 * LOW, 3 * LOW)
                    sub(low_mv[third, :], sx[third, :], low_mv[third, :].bitcast(f32)).then_inc(S["low_lo"], 1)
                    if not last:
                        s_split(g + 1, c * BPC + BPC)
                    dve.wait_ge(S["pe_logit"], g + 1)
                    chain(nc.vector.tensor_copy(lg[:].rearrange("p t e -> p (t e)"), ps[:, S_BANK, 0:TT * NE]))
                    nc.vector.memset(gap[:], 0.0)
                    for t in range(TT):
                        ins = nc.vector.max(top[:, t, :], lg[:, t, :])
                    chain(ins)
                    sub(gap[:], top[:, :, 1:2], top[:, :, 0:1]).then_inc(S["gap_done"], 1)
                    for t in range(TT):
                        ins = nc.vector.max_index(top_i[:, t, :], top[:, t, :], lg[:, t, :])
                    chain(ins)
                    chain(nc.vector.tensor_copy(top_f[:], top_i[:]))
                    chain(nc.vector.tensor_tensor(ma[:], iota_sb[:], top_f[:, :, 0:1].broadcast_to([P, TT, NE]),
                                                  ALU.is_equal), False)
                    chain(nc.vector.tensor_tensor(mb[:], iota_sb[:], top_f[:, :, 1:2].broadcast_to([P, TT, NE]),
                                                  ALU.is_equal), False)
                    dve.wait_ge(S["exp_done"], g + 1)
                    chain(nc.vector.tensor_scalar(den[:], ex[:], 1.0, None, ALU.add))
                    chain(nc.vector.reciprocal(wb[:], den[:]))
                    chain(nc.vector.tensor_scalar(wa[:], wb[:], 2.0, None, ALU.mult))
                    chain(nc.vector.tensor_tensor(den[:], ex[:], wa[:], ALU.mult))
                    chain(nc.vector.tensor_tensor(ma[:], ma[:], wa[:].broadcast_to([P, TT, NE]), ALU.mult), False)
                    chain(nc.vector.tensor_tensor(mb[:], mb[:], den[:].broadcast_to([P, TT, NE]), ALU.mult))
                    nc.vector.tensor_tensor(gates[:].rearrange("p t (e r) -> p (t e) r", r=R),
                                            *(m[:].rearrange("p t e -> p (t e)").unsqueeze(2)
                                              .broadcast_to([P, TT * NE, R]) for m in (ma, mb)),
                                            ALU.add).then_inc(S["gate_done"], 1)
                    dve.wait_ge(S["h_done"], g + (1 + FREE))
                    dve.wait_ge(S["pe_gate"], g + 1)
                    nc.vector.tensor_tensor(hg[:], ps[:, S_BANK, :], h_sb[:], ALU.mult).then_inc(S["hg_done"], 1)
                    dve.wait_ge(S["hg_hi"], g + 1)
                    sub(hg_hl[:, 1, :], hg[:], hg_hl[:, 0, :].bitcast(f32)).then_inc(S["hg_lo"], 1)
                    assert count[0] == CHAIN

                    def finish(ms):
                        for m in ms:
                            dve.wait_ge(S["pe_out"], g * KT + (m + 1))
                            dve.wait_ge(S["resid_done"], g * KT + (m + 1))
                            nc.vector.tensor_tensor(out_st[:, m % SLOTS, :], ps[:, m % 6, :],
                                                    out_st[:, m % SLOTS, :], ALU.add).then_inc(S["out_done"], 1)

                    finish(range(6))
                    if not last:
                        for k in range(KT):
                            x_split(g + 1, k)
                    elif l + 1 < LAYERS:
                        first(l + 1)
                    finish(range(6, KT))

                with dve.Fori(0, NCH - 1) as c:
                    chunk(c, False)
                chunk(NCH - 1, True)

        @block.gpsimd
        def _(pool):
            for l in range(LAYERS):
                if l:
                    for s in range(SLOTS):
                        pool.wait_ge(d_out[s], 16 * (KT // SLOTS) * NCH * l + 16)
                nc.gpsimd.memset(acc[:], 0.0).then_inc(S["acc_zero"], 1)
                pool.wait_ge(S["pe_bias"], NOB * (l + 1))
                with pool.Fori(0, NCH) as c:
                    g = c + NCH * l
                    for m in range(KT):
                        pool.wait_ge(S["x_lo"], g * KT + (m + 1))
                        pool.wait_ge(d_out[m % SLOTS], g * (16 * KT // SLOTS) + 16 * (m // SLOTS) + 16)
                        nc.gpsimd.tensor_tensor(out_st[:, m % SLOTS, :], x_hl[:, m, 0, :].bitcast(f32),
                                                x_hl[:, m, 1, :].bitcast(f32), ALU.add).then_inc(S["resid_done"], 1)


def kernel(**inputs):
    import numpy as np
    import concourse.bacc as bacc
    from concourse.bass_utils import run_bass_kernel_spmd

    a = {k: np.asarray(v) for k, v in inputs.items()}
    rows = np.arange(SROWS)
    router = rows >= STACK
    low = rows < ONES_ROW
    smask = np.stack([np.where(low, rows % LOW // R == j, router) for j in range(BPC)]
                     + [~low & ~router], 1).astype(np.float32)
    rtail = np.zeros((SROWS, NE), np.float32)
    rtail[STACK:] = np.eye(NE)

    def tiles(w):
        return w.reshape(KT, P, KT, P).transpose(2, 1, 0, 3).reshape(KT, P, D)

    def per_adapter(w):
        return w.reshape(-1, KT, P, R).transpose(0, 2, 1, 3).reshape(-1, P, KT * R)

    def extended(w, la, wr):
        return np.concatenate([w.T, la, wr.T], 1)

    arrays = {
        "xT": a["x"].reshape(T, D).T,
        "w0": np.stack([tiles(a["L0_cond_weight"]), tiles(a["L1_cond_base_weight"])]),
        "ext": np.stack([
            extended(a["L0_ffn_W_base"], a["L0_ffn_lora_A"].reshape(ER, D).T, a["L0_ffn_W_router"]),
            extended(a["L1_ffn_base_W"], a["L1_ffn_lora_A"].transpose(1, 0, 2).reshape(D, ER), a["L1_ffn_router_W"]),
        ]),
        "lb": np.stack([a["L0_ffn_lora_B"].transpose(0, 2, 1).reshape(ER, D), a["L1_ffn_lora_B"].reshape(ER, D)]),
        "a_tab": np.concatenate([per_adapter(a["L0_cond_lora_a_weights"].transpose(0, 2, 1)),
                                 per_adapter(a["L1_cond_lora_A_w"].transpose(0, 2, 1))]),
        "b_tab": np.concatenate([per_adapter(a["L0_cond_lora_b_weights"]), per_adapter(a["L1_cond_lora_B_w"])]),
        "scale_tab": np.concatenate([a["L0_cond_scaling_factors"], np.ones(32, np.float32)])[:, None],
        "ids": np.concatenate([a["itok_B_1_7"], a["itok_B_6_15"]])[None],
        "b0": np.stack([a["L0_cond_bias"], a["L1_cond_base_bias"]]).reshape(LAYERS, KT, P).transpose(0, 2, 1),
        "b1": np.stack([np.concatenate([a["L0_ffn_b_base"], np.zeros(EXT - D, np.float32)]),
                        np.zeros(EXT, np.float32)])[:, None],
        "ident": np.eye(P, dtype=np.float32),
        "smask": smask,
        "iota": np.broadcast_to(np.arange(NE, dtype=np.float32), (P, TT, NE)),
        "rtail": rtail,
    }
    arrays = {f"in_{k}": np.ascontiguousarray(v) for k, v in arrays.items()}
    nc = bacc.Bacc("TRN2", target_bir_lowering=False, num_devices=1)
    args = {k[3:]: nc.dram_tensor(k, v.shape, mybir.dt.from_np(v.dtype), kind="ExternalInput").ap()
            for k, v in arrays.items()}
    args["out"] = nc.dram_tensor("out_T", (D, T), mybir.dt.float32, kind="ExternalOutput").ap()
    fused_layers(nc, **args)
    r = run_bass_kernel_spmd(nc, [arrays], core_ids=[0])
    return r.results[0]["out_T"].T.reshape(BATCH, SEQ, D)
```

```python
from contextlib import ExitStack

import concourse.bass as bass
from concourse import mybir

LAYERS = 2
D = 1024
P = 128
KT = D // P
BATCH, SEQ = 8, 256
T = BATCH * SEQ
CH = 512
NCH = T // CH
BPC = CH // SEQ
TT = CH // P
R = 16
NE = 8
ER = NE * R
EXT = D + ER + NE
NOB = -(-EXT // 512)
OBW = -(-EXT // (4 * NOB)) * 4
OB = tuple((o, min(OBW, EXT - o)) for o in range(0, EXT, OBW))
RT = KT + 1
UNITS = RT * NOB
K_ORDER = (5, 6, 7, 4, 0, 1, 2, 3)
LOW = BPC * R
RHI = 2 * LOW
SROWS = RHI + 2 * NE
ONES_ROW = 3 * LOW
STACK = ONES_ROW + 2
HALF = D // 2
FREE = 3
SLOTS = 4
GROUPS = ((0, 1, 2), (3, 4, 5), (6, 7))
CHAIN = 13


def fused_layers(nc, xT, w0, ext, lb, a_tab, b_tab, scale_tab, ids, b0, b1, ident, smask, iota, rtail, out):
    f32, f32r = mybir.dt.float32, mybir.dt.float32r
    ALU = mybir.AluOpType
    ACT = mybir.ActivationFunctionType
    ds = bass.ds

    ctx = ExitStack()
    with ctx:
        sem_names = (
            "d_ids d_const d_w0h d_w0a d_w0b d_lb d_adapt_a d_b d_scale d_b0 d_b1 d_bw d_stack d_bias_rows "
            "w0h_hi w0h_lo w0_hi w0_lo ep_hi ep_lo e_hi e_lo lb_hi lb_lo p_hi p_lo acc_zero acc_half acc_done "
            "bias_r_done bias_hi bias_lo bwr_done router_cols "
            "ones_done mul_done "
            "pe_unit pe_brow pe_bias pe_s pe_h pe_logit pe_gate pe_out pe_xfree "
            "sx_done sxr_done low_hi low_lo h_done shi_done slo_done gap_done exp_done gate_done hg_done hg_hi hg_lo "
            "x_hi x_lo resid_done out_done dve_step"
        ).split()
        S = {n: ctx.enter_context(nc.semaphore(n)) for n in sem_names}
        d_w0 = [S["d_w0a"], S["d_w0b"]]
        d_e = [ctx.enter_context(nc.semaphore(f"d_e{k}")) for k in range(KT)]
        d_ep = [ctx.enter_context(nc.semaphore(f"d_ep{i}")) for i in range(NOB)]
        d_x = [ctx.enter_context(nc.semaphore(f"d_x{i}")) for i in range(SLOTS)]
        d_out = [ctx.enter_context(nc.semaphore(f"d_out{i}")) for i in range(SLOTS)]

        base = -(-nc.sbuf_base // 64) * 64
        at = [base]

        def place(name, shape, dt, offset=None):
            size = 4
            for n in shape[1:]:
                size *= n
            if offset is None:
                offset = at[0]
                at[0] += -(-size // 32) * 32
            return nc.alloc_sbuf_tensor_at(name, shape, dt, offset=offset)

        E_TILE = 2 * EXT * 4
        e_at = at[0]
        e_hl = place("e_hl", [P, KT, 2, EXT], f32r)
        e_raw = place("e_raw", [P, KT, 2, EXT], f32, e_at)
        x_hl = place("x_hl", [P, KT, 2, CH], f32r, e_at)
        lb_hl = place("lb_hl", [P, 2, D], f32r, e_at + 4 * E_TILE)
        lb_raw = place("lb_raw", [P, 2, D], f32, e_at + 4 * E_TILE)
        w0_at = at[0]
        w0_hl = place("w0_hl", [P, 2, 2, D], f32r)
        w0_raw = place("w0_raw", [P, 2, 2, D], f32, w0_at)
        bias_hl = place("bias_hl", [1, 2, EXT], f32r, w0_at)
        p_hl = place("p_hl", [P, KT, 2, EXT], f32r)
        s_hl = place("s_hl", [P, KT, SROWS], f32r)
        a_raw = place("a_raw", [P, BATCH, KT, R], f32)
        stack = place("stack", [STACK, D + ER], f32r)
        out_at = at[0]
        out_st = place("out_st", [P, SLOTS, CH], f32)
        acc = place("acc", [P, EXT], f32, out_at)
        x_at = at[0]
        x_st = place("x_st", [P, SLOTS, CH], f32)
        b_raw = place("b_raw", [P, BATCH, KT, R], f32, x_at)
        misc_at = at[0]
        h_sb = place("h_sb", [P, CH], f32)
        hg_at = at[0]
        hg = place("hg", [P, CH], f32)
        gates = place("gates", [P, TT, ER], f32, hg_at)
        hg_hl = place("hg_hl", [P, 2, CH], f32r)
        low_b = place("low_b", [LOW, CH], f32)
        bw_st = place("bw_st", [P, NOB, 2, OBW], f32r, misc_at)
        sx = place("sx", [SROWS, CH], f32)
        low_mv = place("low_mv", [STACK, CH], f32r)
        ident_sb = place("ident_sb", [P, P], f32)
        iota_sb = place("iota_sb", [P, TT, NE], f32)
        smask_sb = place("smask_sb", [2 * LOW, BPC], f32)
        ones_sb = place("ones_sb", [P, 1], f32)
        scale_sb = place("scale_sb", [2 * LOW, BATCH], f32)
        mul_sb = place("mul_sb", [2 * LOW, BATCH], f32)
        rlog = place("rlog", [SROWS, NE], f32)
        bwr = place("bwr", [P, NE], f32)
        bias_r = place("bias_r", [1, NE], f32)
        b0_sb = place("b0_sb", [P, KT], f32)
        ids_sb = place("ids_sb", [1, LAYERS * BATCH], mybir.dt.int32)
        lg = place("lg", [P, TT, NE], f32)
        top = place("top", [P, TT, 8], f32)
        top_i = place("top_i", [P, TT, 8], mybir.dt.uint32)
        top_f = place("top_f", [P, TT, 8], f32)
        gap = place("gap", [P, TT, 1], f32)
        ex = place("ex", [P, TT, 1], f32)
        den = place("den", [P, TT, 1], f32)
        wa = place("wa", [P, TT, 1], f32)
        wb = place("wb", [P, TT, 1], f32)
        ma = place("ma", [P, TT, NE], f32)
        mb = place("mb", [P, TT, NE], f32)
        assert at[0] <= nc.sbuf_usable_end, at[0] - nc.sbuf_usable_end
        ps = ctx.enter_context(nc.psum_tensor("ps", [P, 8, 512], f32))
        S_BANK, H_BANK = 6, 7

        x1 = nc.dram_tensor("x1_scratch", (D, T), f32, kind="Internal").ap()
        bw_dram = nc.dram_tensor("bw_scratch", (LAYERS, P, 2, EXT), f32, kind="Internal").ap()
        bwr_dram = nc.dram_tensor("bwr_scratch", (LAYERS, P, NE), f32, kind="Internal").ap()
        src_of, dst_of = (xT, x1), (x1, out)

        def fold_bank(odd, ob):
            return (1 - odd) * NOB + ob

        def x_after(k):
            return ((k + 1) * 2 * CH * 4 - 1) // E_TILE + 1

        def by_tile(v):
            return v.rearrange("p (k b r) -> p k b r", k=KT, b=BATCH)

        block = ctx.enter_context(nc.Block())

        @block.sync
        def _(sp):
            def load_first(l):
                if l:
                    sp.wait_ge(S["pe_unit"], UNITS * l)
                    sp.wait_ge(S["d_bias_rows"], 48 * l)
                sp.dma_start(w0_raw[:, 0, 1, HALF:D], w0[l, 0, :, HALF:D]).then_inc(S["d_w0h"], 16)
                k = K_ORDER[0]
                for ob, (o, n) in enumerate(OB):
                    sp.dma_start(e_raw[:, k, 1, o:o + n],
                                 ext[l, k * P:(k + 1) * P, o:o + n]).then_inc(d_ep[ob], 16)
                for k in K_ORDER[1:3]:
                    sp.dma_start(e_raw[:, k, 1, :], ext[l, k * P:(k + 1) * P, :]).then_inc(d_e[k], 16)
                sp.dma_start(w0_raw[:, 1, 1, :], w0[l, 1]).then_inc(d_w0[1], 16)

            def load_fold(l):
                sp.dma_start(w0_raw[:, 0, 1, 0:HALF], w0[l, 0, :, 0:HALF]).then_inc(d_w0[0], 16)
                for k in K_ORDER[3:]:
                    if l and k == 4:
                        sp.wait_ge(S["pe_out"], KT * NCH * l)
                    if l and k == K_ORDER[4]:
                        sp.wait_ge(S["pe_xfree"], KT * NCH * l)
                        sp.wait_ge(S["resid_done"], KT * NCH * l)
                    sp.dma_start(e_raw[:, k, 1, :], ext[l, k * P:(k + 1) * P, :]).then_inc(d_e[k], 16)
                if l == 0:
                    sp.dma_start(ids_sb[:], ids).then_inc(S["d_ids"], 16)
                    for dst, src in ((ident_sb, ident), (iota_sb, iota), (smask_sb, smask), (rlog, rtail)):
                        sp.dma_start(dst[:], src).then_inc(S["d_const"], 16)
                sp.dma_start(b0_sb[:], b0[l]).then_inc(S["d_b0"], 16)
                sp.wait_ge(S["acc_zero"], l + 1)
                sp.dma_start(acc[0:1, :], b1[l]).then_inc(S["d_b1"], 16)

            def load_rows(l):
                with sp.Fori(0, (KT - 2) // 2) as pair:
                    for odd in range(2):
                        sp.wait_ge(S["pe_unit"], pair * (2 * NOB) + (UNITS * l + (1 + odd) * NOB))
                        sp.dma_start(w0_raw[:, odd, 1, :],
                                     w0[l, ds(pair * 2 + (2 + odd), 1)].rearrange("o p n -> (o p) n")
                                     ).then_inc(d_w0[odd], 16)

            def load_x(l, g, c, ks):
                for k in ks:
                    if not (isinstance(g, int) and g * KT + k < SLOTS):
                        sp.wait_ge(S["x_lo"], g * KT + (k - SLOTS + 1))
                    sp.dma_start(x_st[:, k % SLOTS, :],
                                 src_of[l][k * P:(k + 1) * P, ds(c * CH, CH)]).then_inc(d_x[k % SLOTS], 16)

            def store(l, g, c, ms):
                for m in ms:
                    sp.wait_ge(S["out_done"], g * KT + (m + 1 + FREE))
                    sp.dma_start(dst_of[l][m * P:(m + 1) * P, ds(c * CH, CH)],
                                 out_st[:, m % SLOTS, :]).then_inc(d_out[m % SLOTS], 16)

            def load_stack(l, c):
                for i, hl in enumerate((0, 1, 0)):
                    sp.dma_start(stack[i * LOW:(i + 1) * LOW, :].bitcast(f32),
                                 bw_dram[l, ds(c * LOW, LOW), hl, 0:D + ER]).then_inc(S["d_stack"], 16)
                sp.dma_start(rlog[0:LOW, :], bwr_dram[l, ds(c * LOW, LOW), :]).then_inc(S["d_stack"], 16)

            for s in range(SLOTS):
                sp.sem_inc(d_out[s], 16)
            load_first(0)
            for l in range(LAYERS):
                g0 = NCH * l
                load_fold(l)
                load_rows(l)
                sp.wait_ge(S["w0_lo"], RT * (l + 1))
                if l:
                    for s in range(SLOTS):
                        sp.wait_ge(d_out[s], 16 * (KT // SLOTS) * NCH * l + 16)
                load_x(l, g0, 0, range(KT))
                sp.wait_ge(S["pe_brow"], (KT - 1) * l + 5)
                sp.wait_ge(S["acc_done"], KT * l + 5)
                sp.dma_start(lb_raw[:, 1, :], lb[l]).then_inc(S["d_lb"], 16)
                for ob, (o, n) in enumerate(OB):
                    sp.wait_ge(S["p_lo"], UNITS * l + KT * NOB + ob + 1)
                    sp.dma_start(bw_dram[l, :, :, o:o + n],
                                 bw_st[:, ob, :, 0:n].bitcast(f32)).then_inc(S["d_bw"], 16)
                sp.wait_ge(S["bwr_done"], l + 1)
                sp.dma_start(bwr_dram[l], bwr[:]).then_inc(S["d_bw"], 16)
                sp.wait_ge(S["bias_r_done"], l + 1)
                sp.wait_ge(S["bias_lo"], NOB * (l + 1))
                for hl in range(2):
                    sp.dma_start(stack[ONES_ROW + hl:ONES_ROW + hl + 1, :].bitcast(f32),
                                 bias_hl[:, hl, 0:D + ER].bitcast(f32)).then_inc(S["d_bias_rows"], 16)
                sp.dma_start(rlog[LOW:LOW + 1, :], bias_r[:]).then_inc(S["d_bias_rows"], 16)
                sp.wait_ge(S["d_bw"], 64 * (l + 1))
                load_stack(l, 0)

                def chunk(c, last):
                    g = c + g0
                    if last and l + 1 < LAYERS:
                        load_first(l + 1)
                    if not last:
                        load_x(l, g + 1, c + 1, range(SLOTS))
                    store(l, g, c, range(6))
                    if not last:
                        load_x(l, g + 1, c + 1, range(SLOTS, KT))
                        sp.wait_ge(S["pe_out"], g * KT + KT)
                        load_stack(l, c + 1)
                    store(l, g, c, range(6, KT))

                with sp.Fori(0, NCH - 1) as c:
                    chunk(c, False)
                chunk(NCH - 1, True)
            for s in range(SLOTS):
                sp.wait_ge(d_out[s], 16 * (KT // SLOTS) * NCH * LAYERS + 16)

        @block.tensor
        def _(pe):
            def split_product(dst, w_hi, w_lo, m_hi, m_lo, start, stop):
                nc.tensor.matmul(dst, w_hi, m_hi, start=start, stop=False)
                nc.tensor.matmul(dst, w_hi, m_lo, start=False, stop=False)
                return nc.tensor.matmul(dst, w_lo, m_hi, start=False, stop=stop)

            def fold_unit(buf, bank, k, ob, start, stop):
                o, n = OB[ob]
                w = [w0_hl[:, buf, hl, k * P:(k + 1) * P] for hl in range(2)]
                return split_product(ps[:, bank, 0:n], w[0], w[1], e_hl[:, k, 0, o:o + n], e_hl[:, k, 1, o:o + n],
                                     start, stop)

            def row_tile(l, rt, odd):
                pe.wait_ge(S["w0_lo"], rt + (l * RT + 1))
                for ob in range(NOB):
                    pe.wait_ge(S["p_lo"], rt * NOB + (UNITS * l + ob - 2 * NOB + 1))
                    for i, k in enumerate(K_ORDER):
                        last = fold_unit(odd, fold_bank(odd, ob), k, ob, i == 0, i == KT - 1)
                    last.then_inc(S["pe_unit"], 1)

            with pe.Fori(0, LAYERS) as l:
                pe.wait_ge(S["w0h_lo"], l + 1)
                pe.wait_ge(S["out_done"], l * (KT * NCH) + FREE - 2)
                for rt, part in ((0, range(3)), (1, range(3)), (0, range(3, KT)), (1, range(3, KT))):
                    if rt == 1 and part[0] == 0:
                        pe.wait_ge(S["out_done"], l * (KT * NCH) + FREE)
                        pe.wait_ge(S["w0_lo"], RT * l + 1)
                    for i in part:
                        if rt == 0 and i >= 1:
                            pe.wait_ge(S["e_lo"], (KT - 1) * l + i)
                        if rt == 0 and i == 4:
                            pe.wait_ge(S["w0_lo"], RT * l + 2)
                        for ob in range(NOB):
                            if rt == 0 and i == 0:
                                pe.wait_ge(S["ep_lo"], NOB * l + ob + 1)
                            last = fold_unit(rt, fold_bank(rt, ob), K_ORDER[i], ob, i == 0, i == KT - 1)
                            if i == KT - 1:
                                last.then_inc(S["pe_unit"], 1)
                with pe.Fori(0, (KT - 2) // 2) as pair:
                    row_tile(l, pair * 2 + 2, 0)
                    row_tile(l, pair * 2 + 3, 1)
                pe.wait_ge(S["w0_lo"], RT * (l + 1))
                pe.wait_ge(S["p_lo"], UNITS * l + (KT - 1) * NOB)
                for k in range(KT):
                    for ob in range(NOB):
                        last = fold_unit(0, fold_bank(0, ob), k, ob, k == 0, k == KT - 1)
                        if k == KT - 1:
                            last.then_inc(S["pe_unit"], 1)
                    if k < KT - 1:
                        last.then_inc(S["pe_brow"], 1)
                pe.wait_ge(S["acc_done"], KT * (l + 1))
                pe.wait_ge(S["p_lo"], UNITS * l + KT * NOB)
                for ob, (o, n) in enumerate(OB):
                    nc.tensor.matmul(ps[0:1, fold_bank(1, ob), 0:n], ones_sb[:], acc[:, o:o + n],
                                     start=True, stop=True).then_inc(S["pe_bias"], 1)
                with pe.Fori(0, NCH) as c:
                    g = c + NCH * l
                    pe.wait_ge(S["router_cols"], l + 1)
                    pe.wait_ge(S["slo_done"], g + 1)
                    pe.wait_ge(S["hg_done"], g + FREE)
                    for k in range(KT):
                        if k % 2 == 0:
                            pe.wait_ge(S["x_lo"], g * KT + (k + 2))
                        for hl in range(2):
                            last = nc.tensor.matmul(ps[0:SROWS, S_BANK, :], s_hl[:, k, :], x_hl[:, k, hl, :],
                                                    start=(k + hl == 0), stop=(k + hl == KT))
                    last.then_inc(S["pe_s"], 1)
                    pe.wait_ge(S["h_done"], g + FREE)
                    for k in range(KT):
                        split_product(ps[:, H_BANK, :], p_hl[:, k, 0, D:D + ER], p_hl[:, k, 1, D:D + ER],
                                      x_hl[:, k, 0, :], x_hl[:, k, 1, :], k == 0, False)
                    pe.wait_ge(S["low_lo"], g + 1)
                    pe.wait_ge(S["d_stack"], g * 64 + 64)
                    pe.wait_ge(S["d_bias_rows"], 48 * (l + 1))
                    nc.tensor.matmul(ps[:, H_BANK, :], stack[:, D:D + ER], low_mv[:], start=False,
                                     stop=True).then_inc(S["pe_h"], 1)
                    pe.wait_ge(S["sxr_done"], g + 1)
                    pe.wait_ge(S["ones_done"], 1)
                    for t in range(TT):
                        last = nc.tensor.matmul(ps[:, S_BANK, t * NE:(t + 1) * NE], sx[:, t * P:(t + 1) * P],
                                                rlog[:], start=True, stop=True)
                    last.then_inc(S["pe_logit"], 1)

                    def main(group, freeing):
                        for k in range(KT):
                            for m in group:
                                last = split_product(ps[:, m % 6, :], p_hl[:, k, 0, m * P:(m + 1) * P],
                                                     p_hl[:, k, 1, m * P:(m + 1) * P],
                                                     x_hl[:, k, 0, :], x_hl[:, k, 1, :], k == 0, False)
                            if freeing:
                                last.then_inc(S["pe_xfree"], 1)

                    def low_and_experts(group):
                        for m in group:
                            cols = slice(m * P, (m + 1) * P)
                            nc.tensor.matmul(ps[:, m % 6, :], stack[:, cols], low_mv[:], start=False, stop=False)
                            split_product(ps[:, m % 6, :], lb_hl[:, 0, cols], lb_hl[:, 1, cols],
                                          hg_hl[:, 0, :], hg_hl[:, 1, :], False, True).then_inc(S["pe_out"], 1)

                    pe.wait_ge(S["out_done"], g * KT + FREE)
                    pe.wait_ge(S["p_lo"], UNITS * (l + 1))
                    pe.wait_ge(S["bias_lo"], NOB * (l + 1))
                    main(GROUPS[0], False)
                    pe.wait_ge(S["gate_done"], g + 1)
                    for t in range(TT):
                        last = nc.tensor.transpose(ps[:, S_BANK, t * P:(t + 1) * P], gates[:, t, :], ident_sb[:])
                    last.then_inc(S["pe_gate"], 1)
                    main(GROUPS[1], False)
                    pe.wait_ge(S["hg_lo"], g + 1)
                    pe.wait_ge(S["lb_lo"], l + 1)
                    low_and_experts(GROUPS[0])
                    low_and_experts(GROUPS[1])
                    pe.wait_ge(S["out_done"], g * KT + (2 + FREE))
                    main(GROUPS[2], True)
                    low_and_experts(GROUPS[2])

        @block.scalar
        def _(act):
            def w0_split(l, buf, loads):
                act.wait_ge(d_w0[buf], loads)
                nc.scalar.copy(w0_hl[:, buf, 0, :], w0_raw[:, buf, 1, :]).then_inc(S["w0_hi"], 1)

            def e_split(l, i):
                k = K_ORDER[i]
                act.wait_ge(d_e[k], 16 * (l + 1))
                nc.scalar.copy(e_hl[:, k, 0, :], e_raw[:, k, 1, :]).then_inc(S["e_hi"], 1)

            def first(l):
                act.wait_ge(S["d_w0h"], 16 * (l + 1))
                nc.scalar.copy(w0_hl[:, 0, 0, HALF:D], w0_raw[:, 0, 1, HALF:D]).then_inc(S["w0h_hi"], 1)
                k = K_ORDER[0]
                for ob, (o, n) in enumerate(OB):
                    act.wait_ge(d_ep[ob], 16 * (l + 1))
                    nc.scalar.copy(e_hl[:, k, 0, o:o + n], e_raw[:, k, 1, o:o + n]).then_inc(S["ep_hi"], 1)
                for i in range(1, 3):
                    e_split(l, i)
                w0_split(l, 1, 16 * (KT // 2) * l + 16)

            def p_evac(l, rt, odd):
                for ob, (o, n) in enumerate(OB):
                    act.wait_ge(S["pe_unit"], rt * NOB + (UNITS * l + ob + 1))
                    act.reg_add(act_idle, act_idle, 1)
                    nc.scalar.copy(p_hl[:, ds(rt, 1), 0, o:o + n],
                                   ps[:, fold_bank(odd, ob), 0:n].unsqueeze(1)).then_inc(S["p_hi"], 1)

            def step(l, rt, odd):
                p_evac(l, rt, odd)
                w0_split(l, odd, rt * 8 + (16 * (KT // 2) * l + (24 if odd else 32)))

            act.sem_inc(S["h_done"], FREE)
            act_idle = act.alloc_register("act_idle")
            act.reg_mov(act_idle, 0)
            first(0)
            for l in range(LAYERS):
                act.wait_ge(d_w0[0], 16 * (KT // 2) * l + 16)
                nc.scalar.copy(w0_hl[:, 0, 0, 0:HALF], w0_raw[:, 0, 1, 0:HALF]).then_inc(S["w0_hi"], 1)
                for i in range(3, KT):
                    e_split(l, i)

                def s_split(b):
                    nc.scalar.copy(s_hl[:, :, 0:LOW].rearrange("p k (j r) -> p k j r", j=BPC),
                                   a_raw[:, ds(b, BPC), :, :].rearrange("p j k r -> p k j r")
                                   ).then_inc(S["shi_done"], 1)

                step(l, 0, 0)
                step(l, 1, 1)
                with act.Fori(0, 2) as pair:
                    step(l, pair * 2 + 2, 0)
                    step(l, pair * 2 + 3, 1)
                act.wait_ge(S["d_adapt_a"], 16 * BATCH * (l + 1))
                if l:
                    act.wait_ge(S["pe_s"], NCH * l)
                s_split(0)
                p_evac(l, KT - 2, 0)
                act.wait_ge(S["d_b"], 16 * BATCH * (l + 1))
                nc.scalar.copy(by_tile(w0_hl[:, 0, 0, :]),
                               b_raw[:].rearrange("p b k r -> p k b r")).then_inc(S["w0_hi"], 1)
                p_evac(l, KT - 1, 1)

                def x_split(g, k, fresh):
                    act.wait_ge(d_x[k % SLOTS], g * (16 * KT // SLOTS) + 16 * (k // SLOTS + 1))
                    if fresh:
                        act.wait_ge(S["pe_brow"], (KT - 1) * l + x_after(k))
                        act.wait_ge(S["acc_done"], KT * l + x_after(k))
                    else:
                        act.wait_ge(S["pe_xfree"], (g - 1) * KT + (k + 1))
                        act.wait_ge(S["resid_done"], (g - 1) * KT + (k + 1))
                    nc.scalar.copy(x_hl[:, k, 0, :], x_st[:, k % SLOTS, :]).then_inc(S["x_hi"], 1)

                for k in range(KT):
                    x_split(NCH * l, k, True)
                for ob, (o, n) in enumerate(OB):
                    act.wait_ge(S["pe_unit"], UNITS * l + KT * NOB + ob + 1)
                    nc.scalar.copy(bw_st[:, ob, 0, 0:n], ps[:, fold_bank(0, ob), 0:n]).then_inc(S["p_hi"], 1)
                act.wait_ge(S["pe_unit"], UNITS * (l + 1))
                for ob, (o, n) in enumerate(OB):
                    act.wait_ge(S["pe_bias"], NOB * l + ob + 1)
                    nc.scalar.copy(bias_hl[:, 0, o:o + n], ps[0:1, fold_bank(1, ob), 0:n]).then_inc(S["bias_hi"], 1)
                act.wait_ge(S["d_lb"], 16 * (l + 1))
                nc.scalar.copy(lb_hl[:, 0, :], lb_raw[:, 1, :]).then_inc(S["lb_hi"], 1)

                def chunk(c, last):
                    g = c + NCH * l
                    act.wait_ge(S["pe_s"], g + 1)
                    nc.scalar.copy(sx[RHI:SROWS, :], ps[RHI:SROWS, S_BANK, :]).then_inc(S["sxr_done"], 1)
                    act.wait_ge(S["sx_done"], g + 1)
                    for i in range(2):
                        ins = nc.scalar.copy(low_mv[i * LOW:(i + 1) * LOW, :], sx[0:LOW, :])
                    ins.then_inc(S["low_hi"], 1)
                    if not last:
                        s_split(c * BPC + BPC)
                    act.wait_ge(S["pe_h"], g + 1)
                    nc.scalar.copy(h_sb[:], ps[:, H_BANK, :]).then_inc(S["h_done"], 1)
                    act.wait_ge(S["gap_done"], g + 1)
                    nc.scalar.activation(ex[:], gap[:], ACT.Exp).then_inc(S["exp_done"], 1)
                    act.wait_ge(S["hg_done"], g + (1 + FREE))
                    nc.scalar.copy(hg_hl[:, 0, :], hg[:]).then_inc(S["hg_hi"], 1)
                    if not last:
                        for k in range(KT):
                            x_split(g + 1, k, False)

                with act.Fori(0, NCH - 1) as c:
                    chunk(c, False)
                chunk(NCH - 1, True)
                if l + 1 < LAYERS:
                    first(l + 1)

        @block.vector
        def _(dve):
            def sub(dst, a, b):
                return nc.vector.tensor_tensor(dst, a, b, ALU.subtract)

            def w0_split(l, rt, buf):
                dve.wait_ge(S["w0_hi"], rt + (RT * l + 1))
                sub(w0_hl[:, buf, 1, :], w0_raw[:, buf, 1, :],
                    w0_hl[:, buf, 0, :].bitcast(f32)).then_inc(S["w0_lo"], 1)

            def e_split(l, i):
                k = K_ORDER[i]
                dve.wait_ge(S["e_hi"], (KT - 1) * l + i)
                sub(e_hl[:, k, 1, :], e_raw[:, k, 1, :], e_hl[:, k, 0, :].bitcast(f32)).then_inc(S["e_lo"], 1)

            def first(l):
                dve.wait_ge(S["w0h_hi"], l + 1)
                sub(w0_hl[:, 0, 1, HALF:D], w0_raw[:, 0, 1, HALF:D],
                    w0_hl[:, 0, 0, HALF:D].bitcast(f32)).then_inc(S["w0h_lo"], 1)
                k = K_ORDER[0]
                for ob, (o, n) in enumerate(OB):
                    dve.wait_ge(S["ep_hi"], NOB * l + ob + 1)
                    sub(e_hl[:, k, 1, o:o + n], e_raw[:, k, 1, o:o + n],
                        e_hl[:, k, 0, o:o + n].bitcast(f32)).then_inc(S["ep_lo"], 1)
                for i in range(1, 3):
                    e_split(l, i)
                w0_split(l, 0, 1)

            def acc_row(l, k):
                for hl in range(2):
                    if hl:
                        dve.wait_ge(S["acc_half"], k + (KT * l + 1))
                    elif not (isinstance(k, int) and k + KT * l == 0):
                        dve.wait_ge(S["acc_done"], k + KT * l)
                    ins = nc.vector.scalar_tensor_tensor(
                        acc[:].unsqueeze(1), e_hl[:, ds(k, 1), hl, :].bitcast(f32), b0_sb[:, ds(k, 1)],
                        acc[:].unsqueeze(1), op0=ALU.mult, op1=ALU.add)
                    ins.then_inc(S["acc_done" if hl else "acc_half"], 1)

            def p_evac(l, rt, odd):
                for ob, (o, n) in enumerate(OB):
                    dve.wait_ge(S["p_hi"], rt * NOB + (UNITS * l + ob + 1))
                    sub(p_hl[:, ds(rt, 1), 1, o:o + n], ps[:, fold_bank(odd, ob), 0:n].unsqueeze(1),
                        p_hl[:, ds(rt, 1), 0, o:o + n].bitcast(f32)).then_inc(S["p_lo"], 1)

            def step(l, rt, odd):
                acc_row(l, rt - 1)
                p_evac(l, rt, odd)
                w0_split(l, rt + 2, odd)

            dve.sem_inc(S["hg_done"], FREE)
            dve.sem_inc(S["out_done"], FREE)
            nc.vector.memset(ones_sb[:], 1.0)
            nc.vector.memset(sx[:], 1.0)
            nc.vector.memset(low_mv[ONES_ROW:STACK, :].bitcast(f32), 1.0).then_inc(S["ones_done"], 1)
            first(0)
            for l in range(LAYERS):
                dve.wait_ge(S["w0_hi"], RT * l + 2)
                sub(w0_hl[:, 0, 1, 0:HALF], w0_raw[:, 0, 1, 0:HALF],
                    w0_hl[:, 0, 0, 0:HALF].bitcast(f32)).then_inc(S["w0_lo"], 1)
                for i in range(3, KT):
                    e_split(l, i)

                def s_split(g, b):
                    dve.wait_ge(S["shi_done"], g + 1)
                    v = [s_hl[:, :, hl * LOW:(hl + 1) * LOW].rearrange("p k (j r) -> p k j r", j=BPC)
                         for hl in range(2)]
                    sub(v[1], a_raw[:, ds(b, BPC), :, :].rearrange("p j k r -> p k j r"),
                        v[0].bitcast(f32)).then_inc(S["slo_done"], 1)

                dve.wait_ge(S["d_b0"], 16 * (l + 1))
                dve.wait_ge(S["d_b1"], 16 * (l + 1))
                dve.wait_ge(S["e_lo"], (KT - 1) * (l + 1))
                p_evac(l, 0, 0)
                w0_split(l, 2, 0)
                step(l, 1, 1)
                with dve.Fori(0, 2) as pair:
                    step(l, pair * 2 + 2, 0)
                    step(l, pair * 2 + 3, 1)
                s_split(NCH * l, 0)
                dve.wait_ge(S["d_const"], 64)
                dve.wait_ge(S["d_scale"], 16 * BATCH * (l + 1))
                for j in range(BPC):
                    last = nc.vector.tensor_scalar(
                        mul_sb[:].rearrange("p (c j) -> p c j", j=BPC)[:, :, j],
                        scale_sb[:].rearrange("p (c j) -> p c j", j=BPC)[:, :, j],
                        smask_sb[:, j:j + 1], None, ALU.mult)
                last.then_inc(S["mul_done"], 1)
                acc_row(l, KT - 3)
                p_evac(l, KT - 2, 0)
                dve.wait_ge(S["w0_hi"], RT * (l + 1))
                sub(by_tile(w0_hl[:, 0, 1, :]), b_raw[:].rearrange("p b k r -> p k b r"),
                    by_tile(w0_hl[:, 0, 0, :]).bitcast(f32)).then_inc(S["w0_lo"], 1)
                acc_row(l, KT - 2)
                p_evac(l, KT - 1, 1)
                dve.wait_ge(S["p_lo"], UNITS * l + KT * NOB)
                nc.vector.tensor_copy(s_hl[:, :, RHI:SROWS].rearrange("p k (h e) -> p k h e", h=2),
                                      p_hl[:, :, :, D + ER:EXT]).then_inc(S["router_cols"], 1)
                acc_row(l, KT - 1)

                def x_split(g, k):
                    dve.wait_ge(S["x_hi"], g * KT + (k + 1))
                    sub(x_hl[:, k, 1, :], x_st[:, k % SLOTS, :],
                        x_hl[:, k, 0, :].bitcast(f32)).then_inc(S["x_lo"], 1)

                for k in range(KT):
                    x_split(NCH * l, k)
                for ob, (o, n) in enumerate(OB):
                    dve.wait_ge(S["p_hi"], UNITS * l + KT * NOB + ob + 1)
                    sub(bw_st[:, ob, 1, 0:n], ps[:, fold_bank(0, ob), 0:n],
                        bw_st[:, ob, 0, 0:n].bitcast(f32)).then_inc(S["p_lo"], 1)
                n = OB[-1][1]
                nc.vector.tensor_copy(bwr[:], ps[:, fold_bank(0, NOB - 1), n - NE:n]
                                      ).then_inc(S["bwr_done"], 1)
                for ob, (o, n) in enumerate(OB):
                    dve.wait_ge(S["bias_hi"], NOB * l + ob + 1)
                    sub(bias_hl[:, 1, o:o + n], ps[0:1, fold_bank(1, ob), 0:n],
                        bias_hl[:, 0, o:o + n].bitcast(f32)).then_inc(S["bias_lo"], 1)
                nc.vector.tensor_copy(bias_r[:], ps[0:1, fold_bank(1, NOB - 1), n - NE:n]
                                      ).then_inc(S["bias_r_done"], 1)
                dve.wait_ge(S["lb_hi"], l + 1)
                sub(lb_hl[:, 1, :], lb_raw[:, 1, :], lb_hl[:, 0, :].bitcast(f32)).then_inc(S["lb_lo"], 1)
                dve.wait_ge(S["d_bw"], 64 * (l + 1))
                dve.wait_ge(S["mul_done"], l + 1)

                def chunk(c, last):
                    g = c + NCH * l
                    count = [0]

                    def chain(ins, wait=True):
                        ins.then_inc(S["dve_step"], 1)
                        count[0] += 1
                        if wait:
                            dve.wait_ge(S["dve_step"], g * CHAIN + count[0])

                    dve.wait_ge(S["pe_s"], g + 1)
                    halves = [slice(j * SEQ, (j + 1) * SEQ) for j in range(BPC)]
                    for j, half in enumerate(halves):
                        ins = nc.vector.tensor_scalar(low_b[:, half], ps[LOW:2 * LOW, S_BANK, half],
                                                      mul_sb[LOW:2 * LOW, ds(c * BPC + j, 1)], None, ALU.mult)
                    chain(ins)
                    for j, half in enumerate(halves):
                        ins = nc.vector.scalar_tensor_tensor(sx[0:LOW, half], ps[0:LOW, S_BANK, half],
                                                             mul_sb[0:LOW, ds(c * BPC + j, 1)], low_b[:, half],
                                                             op0=ALU.mult, op1=ALU.add)
                    ins.then_inc(S["sx_done"], 1)
                    dve.wait_ge(S["low_hi"], g + 1)
                    sub(low_mv[2 * LOW:ONES_ROW, :], sx[0:LOW, :],
                        low_mv[0:LOW, :].bitcast(f32)).then_inc(S["low_lo"], 1)
                    if not last:
                        s_split(g + 1, c * BPC + BPC)
                    dve.wait_ge(S["pe_logit"], g + 1)
                    chain(nc.vector.tensor_copy(lg[:].rearrange("p t e -> p (t e)"), ps[:, S_BANK, 0:TT * NE]))
                    nc.vector.memset(gap[:], 0.0)
                    for t in range(TT):
                        ins = nc.vector.max(top[:, t, :], lg[:, t, :])
                    chain(ins)
                    sub(gap[:], top[:, :, 1:2], top[:, :, 0:1]).then_inc(S["gap_done"], 1)
                    for t in range(TT):
                        ins = nc.vector.max_index(top_i[:, t, :], top[:, t, :], lg[:, t, :])
                    chain(ins)
                    chain(nc.vector.tensor_copy(top_f[:], top_i[:]))
                    chain(nc.vector.tensor_tensor(ma[:], iota_sb[:], top_f[:, :, 0:1].broadcast_to([P, TT, NE]),
                                                  ALU.is_equal), False)
                    chain(nc.vector.tensor_tensor(mb[:], iota_sb[:], top_f[:, :, 1:2].broadcast_to([P, TT, NE]),
                                                  ALU.is_equal), False)
                    dve.wait_ge(S["exp_done"], g + 1)
                    chain(nc.vector.tensor_scalar(den[:], ex[:], 1.0, None, ALU.add))
                    chain(nc.vector.reciprocal(wb[:], den[:]))
                    chain(nc.vector.tensor_scalar(wa[:], wb[:], 2.0, None, ALU.mult))
                    chain(nc.vector.tensor_tensor(den[:], ex[:], wa[:], ALU.mult))
                    chain(nc.vector.tensor_tensor(ma[:], ma[:], wa[:].broadcast_to([P, TT, NE]), ALU.mult), False)
                    chain(nc.vector.tensor_tensor(mb[:], mb[:], den[:].broadcast_to([P, TT, NE]), ALU.mult))
                    nc.vector.tensor_tensor(gates[:].rearrange("p t (e r) -> p (t e) r", r=R),
                                            *(m[:].rearrange("p t e -> p (t e)").unsqueeze(2)
                                              .broadcast_to([P, TT * NE, R]) for m in (ma, mb)),
                                            ALU.add).then_inc(S["gate_done"], 1)
                    dve.wait_ge(S["h_done"], g + (1 + FREE))
                    dve.wait_ge(S["pe_gate"], g + 1)
                    nc.vector.tensor_tensor(hg[:], ps[:, S_BANK, :], h_sb[:], ALU.mult).then_inc(S["hg_done"], 1)
                    dve.wait_ge(S["hg_hi"], g + 1)
                    sub(hg_hl[:, 1, :], hg[:], hg_hl[:, 0, :].bitcast(f32)).then_inc(S["hg_lo"], 1)
                    assert count[0] == CHAIN

                    def finish(ms):
                        for m in ms:
                            dve.wait_ge(S["pe_out"], g * KT + (m + 1))
                            dve.wait_ge(S["resid_done"], g * KT + (m + 1))
                            nc.vector.tensor_tensor(out_st[:, m % SLOTS, :], ps[:, m % 6, :],
                                                    out_st[:, m % SLOTS, :], ALU.add).then_inc(S["out_done"], 1)

                    finish(range(6))
                    if not last:
                        for k in range(KT):
                            x_split(g + 1, k)
                    elif l + 1 < LAYERS:
                        first(l + 1)
                    finish(range(6, KT))

                with dve.Fori(0, NCH - 1) as c:
                    chunk(c, False)
                chunk(NCH - 1, True)

        @block.gpsimd
        def _(pool):
            for l in range(LAYERS):
                if l:
                    for s in range(SLOTS):
                        pool.wait_ge(d_out[s], 16 * (KT // SLOTS) * NCH * l + 16)
                nc.gpsimd.memset(acc[:], 0.0).then_inc(S["acc_zero"], 1)
                pool.wait_ge(S["e_lo"], (KT - 1) * (l + 1))
                if l == 0:
                    pool.wait_ge(S["d_ids"], 16)
                else:
                    pool.wait_ge(S["slo_done"], NCH * l)
                    pool.wait_ge(S["x_lo"], KT * NCH * l)
                first, count = ((0, 8), (8, 32))[l]
                a_l, b_l, s_l = (tab[first:first + count] for tab in (a_tab, b_tab, scale_tab))
                for b in range(BATCH):
                    who = pool.value_load(ids_sb[0:1, BATCH * l + b:BATCH * l + b + 1], min_val=0, max_val=count - 1)
                    for dst, tab, done in ((a_raw, a_l, "d_adapt_a"), (b_raw, b_l, "d_b")):
                        pool.dma_start(dst[:, b:b + 1, :, :].rearrange("p o k r -> p (o k r)"),
                                       tab[ds(who, 1)].rearrange("o p n -> (o p) n")).then_inc(S[done], 16)
                    pool.dma_start(scale_sb[:, b:b + 1],
                                   s_l[ds(who, 1)].broadcast_to([2 * LOW, 1])).then_inc(S["d_scale"], 16)
                pool.wait_ge(S["pe_bias"], NOB * (l + 1))
                with pool.Fori(0, NCH) as c:
                    g = c + NCH * l
                    for m in range(KT):
                        pool.wait_ge(S["x_lo"], g * KT + (m + 1))
                        pool.wait_ge(d_out[m % SLOTS], g * (16 * KT // SLOTS) + 16 * (m // SLOTS) + 16)
                        nc.gpsimd.tensor_tensor(out_st[:, m % SLOTS, :], x_hl[:, m, 0, :].bitcast(f32),
                                                x_hl[:, m, 1, :].bitcast(f32), ALU.add).then_inc(S["resid_done"], 1)


def kernel(**inputs):
    import numpy as np
    import concourse.bacc as bacc
    from concourse.bass_utils import run_bass_kernel_spmd

    a = {k: np.asarray(v) for k, v in inputs.items()}
    smask = (np.arange(2 * LOW)[:, None] % LOW // R == np.arange(BPC)).astype(np.float32)
    rtail = np.zeros((SROWS, NE), np.float32)
    rtail[RHI:RHI + NE] = rtail[RHI + NE:] = np.eye(NE)

    def tiles(w):
        return w.reshape(KT, P, KT, P).transpose(2, 1, 0, 3).reshape(KT, P, D)

    def per_adapter(w):
        return w.reshape(-1, KT, P, R).transpose(0, 2, 1, 3).reshape(-1, P, KT * R)

    def extended(w, la, wr):
        return np.concatenate([w.T, la, wr.T], 1)

    arrays = {
        "xT": a["x"].reshape(T, D).T,
        "w0": np.stack([tiles(a["L0_cond_weight"]), tiles(a["L1_cond_base_weight"])]),
        "ext": np.stack([
            extended(a["L0_ffn_W_base"], a["L0_ffn_lora_A"].reshape(ER, D).T, a["L0_ffn_W_router"]),
            extended(a["L1_ffn_base_W"], a["L1_ffn_lora_A"].transpose(1, 0, 2).reshape(D, ER), a["L1_ffn_router_W"]),
        ]),
        "lb": np.stack([a["L0_ffn_lora_B"].transpose(0, 2, 1).reshape(ER, D), a["L1_ffn_lora_B"].reshape(ER, D)]),
        "a_tab": np.concatenate([per_adapter(a["L0_cond_lora_a_weights"].transpose(0, 2, 1)),
                                 per_adapter(a["L1_cond_lora_A_w"].transpose(0, 2, 1))]),
        "b_tab": np.concatenate([per_adapter(a["L0_cond_lora_b_weights"]), per_adapter(a["L1_cond_lora_B_w"])]),
        "scale_tab": np.concatenate([a["L0_cond_scaling_factors"], np.ones(32, np.float32)])[:, None],
        "ids": np.concatenate([a["itok_B_1_7"], a["itok_B_6_15"]])[None],
        "b0": np.stack([a["L0_cond_bias"], a["L1_cond_base_bias"]]).reshape(LAYERS, KT, P).transpose(0, 2, 1),
        "b1": np.stack([np.concatenate([a["L0_ffn_b_base"], np.zeros(EXT - D, np.float32)]),
                        np.zeros(EXT, np.float32)])[:, None],
        "ident": np.eye(P, dtype=np.float32),
        "smask": smask,
        "iota": np.broadcast_to(np.arange(NE, dtype=np.float32), (P, TT, NE)),
        "rtail": rtail,
    }
    arrays = {f"in_{k}": np.ascontiguousarray(v) for k, v in arrays.items()}
    nc = bacc.Bacc("TRN2", target_bir_lowering=False, num_devices=1)
    args = {k[3:]: nc.dram_tensor(k, v.shape, mybir.dt.from_np(v.dtype), kind="ExternalInput").ap()
            for k, v in arrays.items()}
    args["out"] = nc.dram_tensor("out_T", (D, T), mybir.dt.float32, kind="ExternalOutput").ap()
    fused_layers(nc, **args)
    r = run_bass_kernel_spmd(nc, [arrays], core_ids=[0])
    return r.results[0]["out_T"].T.reshape(BATCH, SEQ, D)
```
